# Optimizing a Trainium2 kernel written in Bass

```python
import numpy as np
import jax
import jax.numpy as jnp

def _softmax(x, axis=-1):
    return jax.nn.softmax(x, axis=axis)

def _gelu(x):
    return jax.nn.gelu(x, approximate=True)

def _silu(x):
    return jax.nn.silu(x)

def _sigmoid(x):
    return jax.nn.sigmoid(x)

def _layernorm(x, axis=-1, eps=1e-05):
    m = jnp.mean(x, axis=axis, keepdims=True)
    v = jnp.var(x, axis=axis, keepdims=True)
    return (x - m) / jnp.sqrt(v + eps)

def _scatter_add(tgt, idx, src, axis=0):
    return tgt.at[idx].add(src)

def _segment_sum(src, seg, n):
    return jax.ops.segment_sum(src, seg, n)
kernel_name = 'mk_cond_resid_d2_seqx_r2_54c91c'

def setup_inputs(seed: int=0):
    np.random.seed(seed)
    _w = jnp.asarray

    def _rec_inputs():
        import jax
        import jax.numpy as jnp
        _rk = jax.random.key(seed)
        x = -7.109e-05 + 0.9999 * jax.random.normal(jax.random.fold_in(_rk, 1), (8, 1024, 512), jnp.float32)
        _lenS = 1024 - jax.random.randint(jax.random.fold_in(_rk, 7), (8,), 0, max(1, 1024 // 4) + 1, jnp.int32)
        _lenS2 = 1024 - jax.random.randint(jax.random.fold_in(_rk, 8), (8,), 0, max(1, 1024 // 4) + 1, jnp.int32)
        itok_B_0_8 = jax.random.randint(jax.random.fold_in(_rk, 11), (8,), 0, 9, jnp.int32)
        itok_B_0_63 = jax.random.randint(jax.random.fold_in(_rk, 12), (8,), 0, 64, jnp.int32)
        return (x, itok_B_0_8, itok_B_0_63)
    x, itok_B_0_8, itok_B_0_63 = _rec_inputs()

    def _L0_cond_setup():
        import jax, jax.numpy as jnp
        import numpy as np
        LN_EPS = 1e-05
        key = jax.random.key(seed)
        ks = jax.random.split(key, 8)
        B, S, H, A, L = (32, 1024, 512, 128, 10)
        return {'hidden_states': jax.random.normal(ks[0], (B, S, H), dtype=jnp.float32), 'language_ids': jax.random.randint(ks[1], (B,), 0, L, dtype=jnp.int64), 'W1': jax.random.normal(ks[2], (L, H, A), dtype=jnp.float32) * (1.0 / np.sqrt(H)), 'b1': jnp.zeros((L, A), dtype=jnp.float32), 'W2': jax.random.normal(ks[3], (L, A, H), dtype=jnp.float32) * (1.0 / np.sqrt(A)), 'b2': jnp.zeros((L, H), dtype=jnp.float32), 'gamma': jnp.ones((L, H), dtype=jnp.float32), 'beta': jnp.zeros((L, H), dtype=jnp.float32)}
    _L0_cond_all = _L0_cond_setup()
    _L0_cond_in = {k: v for k, v in _L0_cond_all.items() if k in ('W1', 'b1', 'W2', 'b2', 'gamma', 'beta')}
    del _L0_cond_all

    def _L1_cond_setup():
        import jax, jax.numpy as jnp
        import numpy as np
        NUM_CATEGORIES = 64
        INPUT_DIM = 512
        HIDDEN_DIM = 512
        B = 128
        S = 64
        key = jax.random.key(seed)
        kx, kc, kw = jax.random.split(key, 3)
        x = jax.random.normal(kx, (B, S, INPUT_DIM), dtype=jnp.float32)
        cat_ids = jax.random.randint(kc, (B,), 0, NUM_CATEGORIES, dtype=jnp.int32)
        W = 0.02 * jax.random.normal(kw, (NUM_CATEGORIES, INPUT_DIM, HIDDEN_DIM), dtype=jnp.float32)
        b = jnp.zeros((NUM_CATEGORIES, HIDDEN_DIM), dtype=jnp.float32)
        return {'x': x, 'cat_ids': cat_ids, 'W': W, 'b': b}
    _L1_cond_all = _L1_cond_setup()
    _L1_cond_in = {k: v for k, v in _L1_cond_all.items() if k in ('W', 'b')}
    del _L1_cond_all
    return {'x': x, 'itok_B_0_8': itok_B_0_8, 'itok_B_0_63': itok_B_0_63, 'L0_cond_W1': _L0_cond_in['W1'], 'L0_cond_b1': _L0_cond_in['b1'], 'L0_cond_W2': _L0_cond_in['W2'], 'L0_cond_b2': _L0_cond_in['b2'], 'L0_cond_gamma': _L0_cond_in['gamma'], 'L0_cond_beta': _L0_cond_in['beta'], 'L1_cond_W': _L1_cond_in['W'], 'L1_cond_b': _L1_cond_in['b']}

def reference(x, itok_B_0_8, itok_B_0_63, L0_cond_W1, L0_cond_b1, L0_cond_W2, L0_cond_b2, L0_cond_gamma, L0_cond_beta, L1_cond_W, L1_cond_b):
    import jax
    import jax.numpy as jnp

    def _L0_cond_ref(hidden_states, language_ids, W1, b1, W2, b2, gamma, beta):
        import jax, jax.numpy as jnp
        import numpy as np
        LN_EPS = 1e-05
        w1 = W1[language_ids]
        w2 = W2[language_ids]
        h = jnp.einsum('bsh,bha->bsa', hidden_states, w1) + b1[language_ids][:, None, :]
        h = jax.nn.relu(h)
        adapted = jnp.einsum('bsa,bah->bsh', h, w2) + b2[language_ids][:, None, :]
        x = hidden_states + adapted
        mean = jnp.mean(x, axis=-1, keepdims=True)
        var = jnp.mean(jnp.square(x - mean), axis=-1, keepdims=True)
        normed = (x - mean) * jax.lax.rsqrt(var + LN_EPS)
        return normed * gamma[language_ids][:, None, :] + beta[language_ids][:, None, :]

    def _L1_cond_ref(x, cat_ids, W, b):
        import jax, jax.numpy as jnp
        import numpy as np
        NUM_CATEGORIES = 64
        INPUT_DIM = 512
        HIDDEN_DIM = 512
        B = 128
        S = 64
        selected_W = W[cat_ids]
        selected_b = b[cat_ids]
        out = jnp.einsum('bsd,bdh->bsh', x, selected_W) + selected_b[:, None, :]
        return out
    x = x + _L0_cond_ref(x, itok_B_0_8, L0_cond_W1, L0_cond_b1, L0_cond_W2, L0_cond_b2, L0_cond_gamma, L0_cond_beta)
    x = x + _L1_cond_ref(x, itok_B_0_63, L1_cond_W, L1_cond_b)
    return x

_drawn_inputs = setup_inputs


def setup_inputs(seed=0):
    import zlib

    import numpy as np

    out = dict(_drawn_inputs(seed))
    spreads = {'L0_cond_b1': (0.0, 0.1),
     'L0_cond_b2': (0.0, 0.1),
     'L0_cond_gamma': (1.0, 0.2),
     'L0_cond_beta': (0.0, 0.1),
     'L1_cond_b': (0.0, 0.1)}
    factors = {}
    for name, (base, spread) in spreads.items():
        noise = np.random.default_rng([zlib.crc32(name.encode()), seed]).standard_normal(out[name].shape)
        drawn = base * np.exp(spread * noise) if base else spread * noise
        out[name] = jnp.asarray(drawn.astype(out[name].dtype))
    for name, factor in factors.items():
        out[name] = (out[name] * factor).astype(out[name].dtype)
    return out
```

```python
from contextlib import ExitStack

import concourse.bass as bass
from concourse import mybir

P = 128


def cond_resid_kernel(nc, x_rows, x_cols, l0_ids, l1_ids, w1_all, w2_all, b2_all, b1_cols,
                      ln_cols, w_all, b_cols, out_cols):
    f32, f32r, i32 = mybir.dt.float32, mybir.dt.float32r, mybir.dt.int32
    ALU = mybir.AluOpType
    ACT = mybir.ActivationFunctionType
    ds = bass.ds

    SAMPLES = l0_ids.shape[1]
    D = x_rows.shape[1]
    A = w1_all.shape[1]
    ROWS = x_rows.shape[0] // SAMPLES
    KC = D // P
    BLOCK = KC
    NB = BLOCK * P
    TILES = x_rows.shape[0] // P
    PER = ROWS // P
    assert A == P and NB == 512 and PER == 2 * BLOCK and TILES == SAMPLES * PER
    EPS = 1e-05

    PAIR = 2 * PER
    TURNS = 3

    LOAD_COLS, LOAD_ROWS = 10, 6
    SPLIT_X = 6
    UP = 4
    BIAS_ROWS = 2
    DOWN = 0
    NORM = -1
    TURN = -4
    MERGE = -5
    OUT = -8
    FINISH = -9

    def in_range(v, i):
        if isinstance(v, int):
            return 0 <= i < TILES
        assert 0 <= i and i + PAIR * (TURNS - 1) < TILES
        return True

    def run_steps(engine, first, loop, last, step):
        for s in range(first, loop):
            step(0, s)
        with engine.Fori(0, PAIR * (TURNS - 1) + 1, PAIR) as v:
            for s in range(loop, loop + PAIR):
                step(v, s)
        for s in range(loop + PAIR * TURNS, last + 1):
            step(0, s)

    with ExitStack() as ctx:
        def sb(name, shape, dt=f32):
            return ctx.enter_context(nc.sbuf_tensor(name, shape, dt))

        def ps(name):
            return ctx.enter_context(nc.psum_tensor(name, [P, 512], f32))

        def sem(name):
            return ctx.enter_context(nc.semaphore(name))

        XC, XR, WR = 16, 8, 8
        xT = sb("xT", [P, XC, NB])
        xrow = sb("xrow", [P, XR, D])
        xT_hi = sb("xT_hi", [P, KC, NB], f32r)
        xT_lo = sb("xT_lo", [P, KC, NB], f32r)
        hT = sb("hT", [P, NB])
        hT_hi = sb("hT_hi", [P, 2, NB], f32r)
        hT_lo = sb("hT_lo", [P, 2, NB], f32r)
        y = sb("y", [P, WR, D])
        x1T = sb("x1T", [P, WR, NB])
        x1T_hi = sb("x1T_hi", [P, WR, NB], f32r)
        x1T_lo = sb("x1T_lo", [P, WR, NB], f32r)
        w1 = sb("w1", [P, KC, A])
        w2 = sb("w2", [P, D])
        w = sb("w", [P, KC, D])
        w1_hi = sb("w1_hi", [P, 2, KC, A], f32r)
        w1_lo = sb("w1_lo", [P, 2, KC, A], f32r)
        w2_hi = sb("w2_hi", [P, 2, D], f32r)
        w2_lo = sb("w2_lo", [P, 2, D], f32r)
        w_hi = sb("w_hi", [P, 2, KC, D], f32r)
        w_lo = sb("w_lo", [P, 2, KC, D], f32r)
        b2_rows = sb("b2_rows", [P, 2, D])
        b1 = sb("b1", [P, 2])
        gamma_beta = sb("gamma_beta", [P, 2, 2 * KC])
        b = sb("b", [P, 2, KC])
        b_beta = sb("b_beta", [P, 2, KC])
        ident = sb("ident", [P, P])
        ids0 = sb("ids0", [1, SAMPLES], i32)
        ids1 = sb("ids1", [1, SAMPLES], i32)
        eps = sb("eps", [P, 1])
        row_sum = sb("row_sum", [P, WR])
        neg_mean = sb("neg_mean", [P, WR])
        sq_sum = sb("sq_sum", [P, WR])
        std = sb("std", [P, WR])
        neg_half_var = sb("neg_half_var", [P, WR])
        rstd0 = sb("rstd0", [P, WR])
        newton = sb("newton", [P, WR])
        rstd = sb("rstd", [P, WR])
        shift = sb("shift", [P, WR])

        h_ps = ps("h_ps")
        down_ps = [ps(f"down_ps{k}") for k in range(2)]
        turn_ps = [ps(f"turn_ps{k}") for k in range(2)]
        out_ps = [ps(f"out_ps{k}") for k in range(2)]
        square_ps = ps("square_ps")

        ids_in = [sem("ids0_in"), sem("ids1_in")]
        cols_in = [sem(f"cols_in{k}") for k in range(XC)]
        rows_in = [sem(f"rows_in{k}") for k in range(XR)]
        stored = [sem(f"stored{k}") for k in range(WR)]
        w1_in, w2_in, w_in = sem("w1_in"), sem("w2_in"), sem("w_in")
        b1_in = [sem(f"b1_in{k}") for k in range(2)]
        b2_in = [sem(f"b2_in{k}") for k in range(2)]
        gamma_beta_in = [sem(f"gamma_beta_in{k}") for k in range(2)]
        b_in = [sem(f"b_in{k}") for k in range(2)]
        up_done, down_done, turn_done, out_done = (sem(n) for n in ("up_done", "down_done", "turn_done", "out_done"))
        xhi_done, xlo_done = sem("xhi_done"), sem("xlo_done")
        relu_done, hhi_done, hlo_done = sem("relu_done"), sem("hhi_done"), sem("hlo_done")
        rowbias_done, y_done, mean_done, square_done, std_done = (
            sem(n) for n in ("rowbias_done", "y_done", "mean_done", "square_done", "std_done"))
        rstd0_done, newton_done, rstd_done, shift_done, norm_done = (
            sem(n) for n in ("rstd0_done", "newton_done", "rstd_done", "shift_done", "norm_done"))
        x1_done, x1hi_done, x1lo_done, final_done = (
            sem(n) for n in ("x1_done", "x1hi_done", "x1lo_done", "final_done"))
        w1hi_done, w1lo_done, w2hi_done, w2lo_done, whi_done, wlo_done = (
            sem(n) for n in ("w1hi_done", "w1lo_done", "w2hi_done", "w2lo_done", "whi_done", "wlo_done"))
        bbeta_done, ident_zero, ident_done, eps_done = (
            sem(n) for n in ("bbeta_done", "ident_zero", "ident_done", "eps_done"))

        def slot_loads(v, i, slots):
            return (PAIR // slots) * v + 16 * (i // slots + 1)

        def sample_loads(v, m):
            return v + 16 * (m // 2 + 1)

        block = ctx.enter_context(nc.Block())

        @block.sync
        def _(sp):
            sp.dma_start(ids0[:], l0_ids).then_inc(ids_in[0], 16)
            sp.dma_start(ids1[:], l1_ids).then_inc(ids_in[1], 16)
            ids_ready = [False, False]

            def at(v, times, base):
                return base if isinstance(v, int) else sp.snap(v * times + base)

            def sample_row(which, v, m, rows):
                if not ids_ready[which]:
                    sp.wait_ge(ids_in[which], 16)
                    ids_ready[which] = True
                tile, table = ((ids0, w1_all.shape[0] // D), (ids1, w_all.shape[0] // D))[which]
                return sp.snap(sp.value_load(tile[0:1, ds(v // PER + m, 1)], min_val=0, max_val=table - 1) * rows)

            def load_cols(v, i):
                row = at(v, D // PER, (i // PER) * D + (i % KC) * P)
                half = (i // BLOCK) % 2
                if i >= XC:
                    sp.wait_ge(x1_done, v + i - XC + 1)
                sp.dma_start(xT[:, i % XC, :], x_cols[ds(row, P), half * NB:(half + 1) * NB]
                             ).then_inc(cols_in[i % XC], 16)

            def load_rows(v, i):
                row = at(v, P, P * i)
                if i >= XR:
                    sp.wait_ge(y_done, v + i - XR + 1)
                sp.dma_start(xrow[:, i % XR, :], x_rows[ds(row, P), :]).then_inc(rows_in[i % XR], 16)

            def load_w1(v, m):
                row = sample_row(0, v, m, D)
                if m >= 1:
                    sp.wait_ge(w1lo_done, v + PER * m)
                sp.dma_start(w1[:], w1_all[ds(row, D), :].rearrange("(k p) a -> p k a", p=P)).then_inc(w1_in, 16)

            def load_w2(v, m):
                row = sample_row(0, v, m, A)
                if m >= 1:
                    sp.wait_ge(w2lo_done, v + PER * m)
                sp.dma_start(w2[:], w2_all[ds(row, A), :]).then_inc(w2_in, 16)

            def load_w(v, m):
                row = sample_row(1, v, m, D)
                if m >= 1:
                    sp.wait_ge(wlo_done, v + PER * m)
                sp.dma_start(w[:], w_all[ds(row, D), :].rearrange("(k p) n -> p k n", p=P)).then_inc(w_in, 16)

            def load_b1(v, m):
                row = sample_row(0, v, m, P)
                if m >= 2:
                    sp.wait_ge(relu_done, v + PER * (m - 1))
                sp.dma_start(b1[:, m % 2:m % 2 + 1], b1_cols[ds(row, P), :]).then_inc(b1_in[m % 2], 16)

            def load_b2(v, m):
                row = sample_row(0, v, m, 1)
                if m >= 2:
                    sp.wait_ge(rowbias_done, v + PER * (m - 1))
                sp.dma_start(b2_rows[:, m % 2, :], b2_all[ds(row, 1), :].to_broadcast([P, D])
                             ).then_inc(b2_in[m % 2], 16)

            def load_norm(v, m):
                row0, row1 = sample_row(0, v, m, P), sample_row(1, v, m, P)
                if m >= 2:
                    sp.wait_ge(x1lo_done, v + PER * (m - 1))
                sp.dma_start(gamma_beta[:, m % 2, :], ln_cols[ds(row0, P), :]).then_inc(gamma_beta_in[m % 2], 16)
                sp.dma_start(b[:, m % 2, :], b_cols[ds(row1, P), :]).then_inc(b_in[m % 2], 16)

            sample_loads_at = [(load_w1, -10), (load_w2, -9), (load_b1, -8), (load_b2, -6),
                               (load_norm, -3), (load_w, -2)]

            def step(v, s):
                for load, at in sample_loads_at:
                    if (s - at) % PER == 0 and in_range(v, s - at):
                        load(v, (s - at) // PER)
                if in_range(v, s + LOAD_COLS):
                    load_cols(v, s + LOAD_COLS)
                if in_range(v, s + LOAD_ROWS):
                    load_rows(v, s + LOAD_ROWS)

            run_steps(sp, -LOAD_COLS, 6, TILES, step)
            for k in range(WR):
                sp.wait_ge(stored[k], 16 * (TILES // WR))

        @block.scalar
        def _(act):
            act.wait_ge(eps_done, 1)

            def split_cols(v, i):
                act.wait_ge(cols_in[i % XC], slot_loads(v, i, XC))
                if i >= KC:
                    act.wait_ge(up_done, v + i - KC + 1)
                nc.scalar.copy(xT_hi[:, i % KC, :], xT[:, i % XC, :]).then_inc(xhi_done, 1)

            def split_w1(v, m):
                act.wait_ge(w1_in, 2 * v + 16 * (m + 1))
                if m >= 2:
                    act.wait_ge(up_done, v + PER * (m - 1))
                nc.scalar.copy(w1_hi[:, m % 2], w1[:]).then_inc(w1hi_done, PER)

            def split_w2(v, m):
                act.wait_ge(w2_in, 2 * v + 16 * (m + 1))
                if m >= 2:
                    act.wait_ge(down_done, v + PER * (m - 1))
                nc.scalar.copy(w2_hi[:, m % 2], w2[:]).then_inc(w2hi_done, PER)

            def split_w(v, m, k):
                if k == 0:
                    act.wait_ge(w_in, 2 * v + 16 * (m + 1))
                nc.scalar.copy(w_hi[:, m % 2, k], w[:, k]).then_inc(whi_done, PER // KC)

            def relu(v, blk):
                m = blk // 2
                act.wait_ge(up_done, v + BLOCK * (blk + 1))
                if blk % 2 == 0:
                    act.wait_ge(b1_in[m % 2], sample_loads(v, m))
                if blk >= 1:
                    act.wait_ge(hlo_done, v + BLOCK * blk)
                nc.scalar.activation(hT[:], h_ps[:], ACT.Relu, bias=b1[:, m % 2:m % 2 + 1]
                                     ).then_inc(relu_done, BLOCK)
                act.wait_ge(relu_done, v + BLOCK * (blk + 1))
                if blk >= 2:
                    act.wait_ge(down_done, v + BLOCK * (blk - 1))
                nc.scalar.copy(hT_hi[:, blk % 2, :], hT[:]).then_inc(hhi_done, BLOCK)

            def square(v, i):
                r = slice(i % WR, i % WR + 1)
                act.wait_ge(mean_done, v + i + 1)
                if i >= 1:
                    act.wait_ge(square_done, v + i)
                nc.scalar.activation(square_ps[:], y[:, i % WR, :], ACT.Square, bias=neg_mean[:, r],
                                     accum_out=sq_sum[:, r]).then_inc(square_done, 1)
                act.wait_ge(square_done, v + i + 1)
                nc.scalar.activation(std[:, r], sq_sum[:, r], ACT.Sqrt, bias=eps[:], scale=1.0 / D
                                     ).then_inc(std_done, 1)

            def normalise(v, i):
                r = slice(i % WR, i % WR + 1)
                act.wait_ge(shift_done, v + i + 1)
                nc.scalar.activation(y[:, i % WR, :], y[:, i % WR, :], ACT.Identity, bias=shift[:, r],
                                     scale=rstd[:, r]).then_inc(norm_done, 1)

            def split_x1(v, i):
                beta = KC + i % KC
                act.wait_ge(x1_done, v + i + 1)
                nc.scalar.activation(x1T_hi[:, i % WR, :], x1T[:, i % WR, :], ACT.Identity,
                                     bias=gamma_beta[:, (i // PER) % 2, beta:beta + 1]).then_inc(x1hi_done, 1)

            def store(v, i):
                act.wait_ge(final_done, v + i + 1)
                first = (i // PER) * D + (i % KC) * P
                half = (i // BLOCK) % 2
                act.dma_start(out_cols[ds(D // PER * v + first, P), half * NB:(half + 1) * NB],
                              x1T[:, i % WR, :]).then_inc(stored[i % WR], 16)

            def step(v, s):
                u = s % PER
                m = s // PER
                if in_range(v, s + SPLIT_X):
                    split_cols(v, s + SPLIT_X)
                if in_range(v, s + MERGE):
                    split_x1(v, s + MERGE)
                if s % BLOCK == BLOCK - 1 and in_range(v, s + 1):
                    relu(v, (s + 1) // BLOCK)
                if in_range(v, s + DOWN):
                    square(v, s + DOWN)
                if in_range(v, s + NORM):
                    normalise(v, s + NORM)
                if u == 1 and in_range(v, (m + 1) * PER):
                    split_w1(v, m + 1)
                if u == 2 and in_range(v, (m + 1) * PER):
                    split_w2(v, m + 1)
                if 3 <= u < 3 + KC and in_range(v, m * PER):
                    split_w(v, m, u - 3)
                if in_range(v, s + FINISH):
                    store(v, s + FINISH)

            run_steps(act, -PER, 9, TILES - 1 - FINISH, step)

        @block.vector
        def _(dve):
            nc.vector.memset(eps[:], EPS).then_inc(eps_done, 1)

            def add_rows(v, i):
                r = slice(i % WR, i % WR + 1)
                dve.wait_ge(down_done, v + i + 1)
                dve.wait_ge(rowbias_done, v + i + 1)
                if i >= WR:
                    dve.wait_ge(turn_done, v + BLOCK * (i // BLOCK - 1))
                nc.vector.scalar_tensor_tensor(y[:, i % WR, :], down_ps[i % 2][:], 1.0, xrow[:, i % XR, :],
                                               ALU.mult, ALU.add, accum_out=row_sum[:, r]).then_inc(y_done, 1)

            def mean(v, i):
                r = slice(i % WR, i % WR + 1)
                dve.wait_ge(y_done, v + i + 1)
                nc.vector.tensor_scalar(neg_mean[:, r], row_sum[:, r], -1.0 / D, None, ALU.mult
                                        ).then_inc(mean_done, 1)

            def rstd_start(v, i):
                r = slice(i % WR, i % WR + 1)
                dve.wait_ge(std_done, v + i + 1)
                nc.vector.tensor_scalar(neg_half_var[:, r], sq_sum[:, r], -0.5 / D, -0.5 * EPS,
                                        ALU.mult, ALU.add)
                nc.vector.reciprocal(rstd0[:, r], std[:, r]).then_inc(rstd0_done, 1)

            def rstd_newton(v, i):
                r = slice(i % WR, i % WR + 1)
                dve.wait_ge(rstd0_done, v + i + 1)
                nc.vector.scalar_tensor_tensor(newton[:, r], rstd0[:, r], neg_half_var[:, r], rstd0[:, r],
                                               ALU.mult, ALU.mult).then_inc(newton_done, 1)

            def rstd_end(v, i):
                r = slice(i % WR, i % WR + 1)
                dve.wait_ge(newton_done, v + i + 1)
                nc.vector.scalar_tensor_tensor(rstd[:, r], newton[:, r], 1.5, rstd0[:, r],
                                               ALU.add, ALU.mult).then_inc(rstd_done, 1)

            def mean_shift(v, i):
                r = slice(i % WR, i % WR + 1)
                dve.wait_ge(rstd_done, v + i + 1)
                nc.vector.tensor_tensor(shift[:, r], neg_mean[:, r], rstd[:, r], ALU.mult
                                        ).then_inc(shift_done, 1)

            def merge(v, i):
                gamma = i % KC
                dve.wait_ge(turn_done, v + i + 1)
                if i % PER == 0:
                    dve.wait_ge(gamma_beta_in[(i // PER) % 2], sample_loads(v, i // PER))
                if i >= WR:
                    dve.wait_ge(stored[i % WR], (PAIR // WR) * v + 16 * (i // WR))
                nc.vector.scalar_tensor_tensor(x1T[:, i % WR, :], turn_ps[i % 2][:],
                                               gamma_beta[:, (i // PER) % 2, gamma:gamma + 1],
                                               xT[:, i % XC, :], ALU.mult, ALU.add).then_inc(x1_done, 1)

            def split_x1(v, i):
                beta = KC + i % KC
                dve.wait_ge(x1hi_done, v + i + 1)
                nc.vector.scalar_tensor_tensor(x1T_lo[:, i % WR, :], x1T[:, i % WR, :],
                                               gamma_beta[:, (i // PER) % 2, beta:beta + 1],
                                               x1T_hi[:, i % WR, :].bitcast(f32),
                                               ALU.add, ALU.subtract).then_inc(x1lo_done, 1)

            def bias_beta(v, m):
                dve.wait_ge(b_in[m % 2], sample_loads(v, m))
                nc.vector.tensor_tensor(b_beta[:, m % 2, :], b[:, m % 2, :], gamma_beta[:, m % 2, KC:],
                                        ALU.add).then_inc(bbeta_done, PER)

            def finish(v, i):
                c = i % KC
                dve.wait_ge(out_done, v + i + 1)
                if i % PER == 0:
                    dve.wait_ge(bbeta_done, v + i + PER)
                nc.vector.scalar_tensor_tensor(x1T[:, i % WR, :], out_ps[i % 2][:],
                                               b_beta[:, (i // PER) % 2, c:c + 1], x1T[:, i % WR, :],
                                               ALU.add, ALU.add).then_inc(final_done, 1)

            def step(v, s):
                if s % PER == 0 and in_range(v, s - PER):
                    bias_beta(v, s // PER - 1)
                if in_range(v, s + NORM):
                    rstd_start(v, s + NORM)
                if in_range(v, s + MERGE):
                    merge(v, s + MERGE)
                if in_range(v, s + NORM):
                    rstd_newton(v, s + NORM)
                if in_range(v, s + DOWN):
                    add_rows(v, s + DOWN)
                if in_range(v, s + NORM):
                    rstd_end(v, s + NORM)
                if in_range(v, s + MERGE):
                    split_x1(v, s + MERGE)
                if in_range(v, s + DOWN):
                    mean(v, s + DOWN)
                if in_range(v, s + NORM):
                    mean_shift(v, s + NORM)
                if in_range(v, s + FINISH):
                    finish(v, s + FINISH)

            run_steps(dve, 0, 14, TILES - 1 - FINISH, step)

        @block.gpsimd
        def _(pool):
            nc.gpsimd.memset(ident[:], 0.0).then_inc(ident_zero, 1)
            pool.wait_ge(ident_zero, 1)
            nc.gpsimd.affine_select(out=ident[:], in_=ident[:], compare_op=ALU.not_equal, fill=1.0, base=0,
                                    pattern=[[-1, P]], channel_multiplier=1).then_inc(ident_done, 1)

            def split_cols(v, i):
                pool.wait_ge(xhi_done, v + i + 1)
                nc.gpsimd.tensor_tensor(xT_lo[:, i % KC, :], xT[:, i % XC, :],
                                        xT_hi[:, i % KC, :].bitcast(f32), ALU.subtract).then_inc(xlo_done, 1)

            def bias_rows(v, i):
                m = i // PER
                pool.wait_ge(rows_in[i % XR], slot_loads(v, i, XR))
                if i % PER == 0:
                    pool.wait_ge(b2_in[m % 2], sample_loads(v, m))
                nc.gpsimd.tensor_tensor(xrow[:, i % XR, :], xrow[:, i % XR, :], b2_rows[:, m % 2, :],
                                        ALU.add).then_inc(rowbias_done, 1)

            def split_h(v, blk):
                pool.wait_ge(hhi_done, v + BLOCK * (blk + 1))
                nc.gpsimd.tensor_tensor(hT_lo[:, blk % 2, :], hT[:], hT_hi[:, blk % 2, :].bitcast(f32),
                                        ALU.subtract).then_inc(hlo_done, BLOCK)

            def split_w1(v, m):
                pool.wait_ge(w1hi_done, v + PER * (m + 1))
                nc.gpsimd.tensor_tensor(w1_lo[:, m % 2], w1[:], w1_hi[:, m % 2].bitcast(f32),
                                        ALU.subtract).then_inc(w1lo_done, PER)

            def split_w2(v, m):
                pool.wait_ge(w2hi_done, v + PER * (m + 1))
                nc.gpsimd.tensor_tensor(w2_lo[:, m % 2], w2[:], w2_hi[:, m % 2].bitcast(f32),
                                        ALU.subtract).then_inc(w2lo_done, PER)

            def split_w(v, m, k):
                pool.wait_ge(whi_done, v + PER * m + PER // KC * (k + 1))
                nc.gpsimd.tensor_tensor(w_lo[:, m % 2, k], w[:, k], w_hi[:, m % 2, k].bitcast(f32),
                                        ALU.subtract).then_inc(wlo_done, PER // KC)

            def step(v, s):
                u = s % PER
                m = s // PER
                if in_range(v, s + SPLIT_X):
                    split_cols(v, s + SPLIT_X)
                if s % BLOCK == BLOCK - 1 and in_range(v, s + 1):
                    split_h(v, (s + 1) // BLOCK)
                if in_range(v, s + BIAS_ROWS):
                    bias_rows(v, s + BIAS_ROWS)
                if u == 1 and in_range(v, (m + 1) * PER):
                    split_w1(v, m + 1)
                if u == 2 and in_range(v, (m + 1) * PER):
                    split_w2(v, m + 1)
                if 3 <= u < 3 + KC and in_range(v, m * PER):
                    split_w(v, m, u - 3)

            run_steps(pool, -PER, 9, TILES - 1, step)

        @block.tensor
        def _(pe):
            def product(out, terms, first=True, last=True):
                for n, (lhsT, rhs) in enumerate(terms):
                    mm = nc.tensor.matmul(out, lhsT, rhs, start=first and n == 0,
                                          stop=last and n == len(terms) - 1)
                return mm

            def up(v, i):
                k, m = i % KC, i // PER
                pe.wait_ge(xlo_done, v + i + 1)
                if i % PER == 0:
                    pe.wait_ge(w1lo_done, v + i + PER)
                if k == 0 and i >= BLOCK:
                    pe.wait_ge(relu_done, v + i)
                hi, lo = w1_hi[:, m % 2, k], w1_lo[:, m % 2, k]
                product(h_ps[:], [(hi, xT_hi[:, k]), (lo, xT_hi[:, k]), (hi, xT_lo[:, k])],
                        first=k == 0, last=k == KC - 1).then_inc(up_done, 1)

            def down(v, i):
                blk, m = i // BLOCK, i // PER
                rows = slice((i % BLOCK) * P, (i % BLOCK + 1) * P)
                if i % BLOCK == 0:
                    pe.wait_ge(hlo_done, v + BLOCK * (blk + 1))
                if i % PER == 0:
                    pe.wait_ge(w2lo_done, v + i + PER)
                if i >= 2:
                    pe.wait_ge(y_done, v + i - 1)
                hi, lo = hT_hi[:, blk % 2, rows], hT_lo[:, blk % 2, rows]
                product(down_ps[i % 2][:], [(hi, w2_hi[:, m % 2]), (hi, w2_lo[:, m % 2]), (lo, w2_hi[:, m % 2])]
                        ).then_inc(down_done, 1)

            def turn(v, i):
                k, blk = i % KC, i // BLOCK
                if k == 0:
                    pe.wait_ge(norm_done, v + BLOCK * (blk + 1))
                if i >= 2:
                    pe.wait_ge(x1_done, v + i - 1)
                for t in range(BLOCK):
                    mm = nc.tensor.transpose(turn_ps[i % 2][:, t * P:(t + 1) * P],
                                             y[:, (blk * BLOCK + t) % WR, k * P:(k + 1) * P], ident[:])
                mm.then_inc(turn_done, 1)

            def out(v, i):
                j, blk, m = i % KC, i // BLOCK, i // PER
                if j == 0:
                    pe.wait_ge(x1hi_done, v + BLOCK * (blk + 1))
                if i % PER == 0:
                    pe.wait_ge(wlo_done, v + i + PER)
                if i >= 2:
                    pe.wait_ge(final_done, v + i - 1)
                cols = slice(j * P, (j + 1) * P)
                x1 = [(blk * BLOCK + k) % WR for k in range(KC)]
                product(out_ps[i % 2][:], [(part[:, m % 2, k, cols], x1T_hi[:, x1[k]])
                                           for k in range(KC) for part in (w_hi, w_lo)], last=False)
                if j == 0:
                    pe.wait_ge(x1lo_done, v + BLOCK * (blk + 1))
                product(out_ps[i % 2][:], [(w_hi[:, m % 2, k, cols], x1T_lo[:, x1[k]]) for k in range(KC)],
                        first=False).then_inc(out_done, 1)

            def step(v, s):
                if in_range(v, s + DOWN):
                    down(v, s + DOWN)
                if in_range(v, s + UP):
                    up(v, s + UP)
                if in_range(v, s + OUT):
                    out(v, s + OUT)
                if s + TURN == 0:
                    pe.wait_ge(ident_done, 1)
                if in_range(v, s + TURN):
                    turn(v, s + TURN)

            run_steps(pe, -UP, 12, TILES - 1 - OUT, step)


def kernel(x, itok_B_0_8, itok_B_0_63, L0_cond_W1, L0_cond_b1, L0_cond_W2, L0_cond_b2, L0_cond_gamma,
           L0_cond_beta, L1_cond_W, L1_cond_b):
    import numpy as np
    import concourse.bacc as bacc
    from concourse.bass_utils import run_bass_kernel_spmd

    x, W1, W2, W = (np.asarray(a) for a in (x, L0_cond_W1, L0_cond_W2, L1_cond_W))
    S, R, D = x.shape

    def columns(a):
        a = np.asarray(a)
        return a.reshape(a.shape[0], -1, P).transpose(0, 2, 1).reshape(a.shape[0] * P, -1)

    arrays = {
        "x_rows": x.reshape(S * R, D),
        "x_cols": x.transpose(0, 2, 1).reshape(S * D, R),
        "l0_ids": np.asarray(itok_B_0_8).reshape(1, S),
        "l1_ids": np.asarray(itok_B_0_63).reshape(1, S),
        "w1_all": W1.reshape(-1, W1.shape[-1]),
        "w2_all": W2.reshape(-1, D),
        "b2_all": np.asarray(L0_cond_b2),
        "b1_cols": columns(L0_cond_b1),
        "ln_cols": np.concatenate([columns(L0_cond_gamma), columns(L0_cond_beta)], axis=1),
        "w_all": W.reshape(-1, D),
        "b_cols": columns(L1_cond_b),
    }
    arrays = {n: np.ascontiguousarray(a) for n, a in arrays.items()}
    nc = bacc.Bacc("TRN2", target_bir_lowering=False, num_devices=1)
    args = [nc.dram_tensor(n, a.shape, mybir.dt.from_np(a.dtype), kind="ExternalInput").ap()
            for n, a in arrays.items()]
    out = nc.dram_tensor("out_cols", (S * D, R), mybir.dt.float32, kind="ExternalOutput").ap()
    cond_resid_kernel(nc, *args, out)
    r = run_bass_kernel_spmd(nc, [arrays], core_ids=[0])
    got = r.results[0]["out_cols"]
    return np.ascontiguousarray(got.reshape(S, D, R).transpose(0, 2, 1))
```

```python
from contextlib import ExitStack

import concourse.bass as bass
from concourse import mybir

P = 128


def cond_resid_kernel(nc, x_rows, x_cols, l0_ids, l1_ids, w1_all, w2_all, b2_all, b1_cols,
                      ln_cols, w_all, b_cols, out_cols):
    f32, f32r, i32 = mybir.dt.float32, mybir.dt.float32r, mybir.dt.int32
    ALU = mybir.AluOpType
    ACT = mybir.ActivationFunctionType
    ds = bass.ds

    SAMPLES = l0_ids.shape[1]
    D = x_rows.shape[1]
    A = w1_all.shape[1]
    ROWS = x_rows.shape[0] // SAMPLES
    KC = D // P
    BLOCK = KC
    NB = BLOCK * P
    TILES = x_rows.shape[0] // P
    PER = ROWS // P
    assert A == P and NB == 512 and PER == 2 * BLOCK and TILES == SAMPLES * PER
    EPS = 1e-05

    PAIR = 2 * PER
    TURNS = 3

    LOAD_COLS, LOAD_ROWS = 10, 6
    SPLIT_X, SPLIT_X_LO = 7, 6
    UP = 5
    BIAS_ROWS = 3
    DOWN = 0
    NORM = -1
    TURN = -4
    MERGE = -5
    OUT = -8
    FINISH = -9

    FIRST_SPLITS = 12
    FIRST_H_SPLITS = {-1: 0, 2: 1}

    def in_range(v, i):
        if isinstance(v, int):
            return 0 <= i < TILES
        assert 0 <= i and i + PAIR * (TURNS - 1) < TILES
        return True

    WEIGHT_PARTS = {1: [("w1", 1, 0)], 2: [("w2", 1, 0)], **{3 + k: [("w", 0, k)] for k in range(KC)}}
    FIRST_WEIGHT_PARTS = {0: [("w1", 1, 0)], 2: [("w", 0, 0)], 3: [("w", 0, 1)], 4: [("w", 0, 2)],
                          5: [("w", 0, 3), ("w2", 1, 0)]}

    def weight_parts(v, s):
        first = 0 <= s < PER
        parts = FIRST_WEIGHT_PARTS if first else WEIGHT_PARTS
        return [(table, s // PER + ahead, k) for table, ahead, k in parts.get(s % PER, [])
                if in_range(v, (s // PER + ahead) * PER)]

    def run_steps(engine, first, loop, last, step):
        for s in range(first, loop):
            step(0, s)
        with engine.Fori(0, PAIR * (TURNS - 1) + 1, PAIR) as v:
            for s in range(loop, loop + PAIR):
                step(v, s)
        for s in range(loop + PAIR * TURNS, last + 1):
            step(0, s)

    with ExitStack() as ctx:
        def sb(name, shape, dt=f32):
            return ctx.enter_context(nc.sbuf_tensor(name, shape, dt))

        def ps(name):
            return ctx.enter_context(nc.psum_tensor(name, [P, 512], f32))

        def sem(name):
            return ctx.enter_context(nc.semaphore(name))

        XC, XR, WR = 16, 8, 8
        xT = sb("xT", [P, XC, NB])
        xrow = sb("xrow", [P, XR, D])
        xT_hi = sb("xT_hi", [P, KC, NB], f32r)
        xT_lo = sb("xT_lo", [P, KC, NB], f32r)
        hT = sb("hT", [P, NB])
        hT_hi = sb("hT_hi", [P, 2, NB], f32r)
        hT_lo = sb("hT_lo", [P, 2, NB], f32r)
        y = sb("y", [P, WR, D])
        x1T = sb("x1T", [P, WR, NB])
        x1T_hi = sb("x1T_hi", [P, WR, NB], f32r)
        x1T_lo = sb("x1T_lo", [P, WR, NB], f32r)
        w1 = sb("w1", [P, KC, A])
        w2 = sb("w2", [P, D])
        w = sb("w", [P, KC, D])
        w1_hi = sb("w1_hi", [P, 2, KC, A], f32r)
        w1_lo = sb("w1_lo", [P, 2, KC, A], f32r)
        w2_hi = sb("w2_hi", [P, 2, D], f32r)
        w2_lo = sb("w2_lo", [P, 2, D], f32r)
        w_hi = sb("w_hi", [P, 2, KC, D], f32r)
        w_lo = sb("w_lo", [P, 2, KC, D], f32r)
        b2_rows = sb("b2_rows", [P, 2, D])
        b1 = sb("b1", [P, 2])
        gamma_beta = sb("gamma_beta", [P, 2, 2 * KC])
        b = sb("b", [P, 2, KC])
        b_beta = sb("b_beta", [P, 2, KC])
        ident = sb("ident", [P, P])
        ids0 = sb("ids0", [1, SAMPLES], i32)
        ids1 = sb("ids1", [1, SAMPLES], i32)
        eps = sb("eps", [P, 1])
        row_sum = sb("row_sum", [P, WR])
        neg_mean = sb("neg_mean", [P, WR])
        sq_sum = sb("sq_sum", [P, WR])
        std = sb("std", [P, WR])
        neg_half_var = sb("neg_half_var", [P, WR])
        rstd0 = sb("rstd0", [P, WR])
        newton = sb("newton", [P, WR])
        rstd = sb("rstd", [P, WR])
        shift = sb("shift", [P, WR])

        h_ps = ps("h_ps")
        down_ps = [ps(f"down_ps{k}") for k in range(2)]
        turn_ps = [ps(f"turn_ps{k}") for k in range(2)]
        out_ps = [ps(f"out_ps{k}") for k in range(2)]
        square_ps = ps("square_ps")

        ids_in = [sem("ids0_in"), sem("ids1_in")]
        cols_in = [sem(f"cols_in{k}") for k in range(XC)]
        rows_in = [sem(f"rows_in{k}") for k in range(XR)]
        stored = [sem(f"stored{k}") for k in range(WR)]
        w1_in, w2_in, w_in = sem("w1_in"), sem("w2_in"), sem("w_in")
        b1_in = [sem(f"b1_in{k}") for k in range(2)]
        b2_in = [sem(f"b2_in{k}") for k in range(2)]
        gamma_beta_in = [sem(f"gamma_beta_in{k}") for k in range(2)]
        b_in = [sem(f"b_in{k}") for k in range(2)]
        up_done, down_done, turn_done, out_done = (sem(n) for n in ("up_done", "down_done", "turn_done", "out_done"))
        first_xhi_done, xhi_done, xlo_done = sem("first_xhi_done"), sem("xhi_done"), sem("xlo_done")
        relu_done, hhi_done, hlo_done = sem("relu_done"), sem("hhi_done"), sem("hlo_done")
        rowbias_done, y_done, mean_done, square_done, std_done = (
            sem(n) for n in ("rowbias_done", "y_done", "mean_done", "square_done", "std_done"))
        rstd0_done, newton_done, rstd_done, shift_done, norm_done = (
            sem(n) for n in ("rstd0_done", "newton_done", "rstd_done", "shift_done", "norm_done"))
        x1_done, x1hi_done, x1lo_done, final_done = (
            sem(n) for n in ("x1_done", "x1hi_done", "x1lo_done", "final_done"))
        w1hi_done, w1lo_done, w2hi_done, w2lo_done, whi_done, wlo_done = (
            sem(n) for n in ("w1hi_done", "w1lo_done", "w2hi_done", "w2lo_done", "whi_done", "wlo_done"))
        warmed_up = sem("warmed_up")
        bbeta_done, ident_zero, ident_done, eps_done, table_loaded = (
            sem(n) for n in ("bbeta_done", "ident_zero", "ident_done", "eps_done", "table_loaded"))

        def slot_loads(v, i, slots):
            return (PAIR // slots) * v + 16 * (i // slots + 1)

        def sample_loads(v, m):
            return v + 16 * (m // 2 + 1)

        block = ctx.enter_context(nc.Block())

        @block.sync
        def _(sp):
            ids_ready = [False, False]

            def at(v, times, base):
                return base if isinstance(v, int) else sp.snap(v * times + base)

            def sample_row(which, v, m, rows):
                if not ids_ready[which]:
                    sp.wait_ge(ids_in[which], 16)
                    ids_ready[which] = True
                tile, table = ((ids0, w1_all.shape[0] // D), (ids1, w_all.shape[0] // D))[which]
                return sp.snap(sp.value_load(tile[0:1, ds(v // PER + m, 1)], min_val=0, max_val=table - 1) * rows)

            def load_cols(v, i):
                row = at(v, D // PER, (i // PER) * D + (i % KC) * P)
                half = (i // BLOCK) % 2
                if i >= XC:
                    sp.wait_ge(x1_done, v + i - XC + 1)
                sp.dma_start(xT[:, i % XC, :], x_cols[ds(row, P), half * NB:(half + 1) * NB]
                             ).then_inc(cols_in[i % XC], 16)

            def load_rows(v, i):
                row = at(v, P, P * i)
                if i >= XR:
                    sp.wait_ge(y_done, v + i - XR + 1)
                sp.dma_start(xrow[:, i % XR, :], x_rows[ds(row, P), :]).then_inc(rows_in[i % XR], 16)

            def load_w1(v, m):
                row = sample_row(0, v, m, D)
                if m >= 1:
                    sp.wait_ge(w1lo_done, v + PER * m)
                sp.dma_start(w1[:], w1_all[ds(row, D), :].rearrange("(k p) a -> p k a", p=P)).then_inc(w1_in, 16)

            def load_w2(v, m):
                row = sample_row(0, v, m, A)
                if m >= 1:
                    sp.wait_ge(w2lo_done, v + PER * m)
                sp.dma_start(w2[:], w2_all[ds(row, A), :]).then_inc(w2_in, 16)

            def load_w(v, m):
                row = sample_row(1, v, m, D)
                if m >= 1:
                    sp.wait_ge(wlo_done, v + PER * m)
                sp.dma_start(w[:], w_all[ds(row, D), :].rearrange("(k p) n -> p k n", p=P)).then_inc(w_in, 16)

            def load_ids0(v, m):
                sp.dma_start(ids0[:], l0_ids).then_inc(ids_in[0], 16)

            def load_ids1(v, m):
                sp.dma_start(ids1[:], l1_ids).then_inc(ids_in[1], 16)

            def load_b1(v, m):
                row = sample_row(0, v, m, P)
                if m >= 2:
                    sp.wait_ge(relu_done, v + PER * (m - 1))
                sp.dma_start(b1[:, m % 2:m % 2 + 1], b1_cols[ds(row, P), :]).then_inc(b1_in[m % 2], 16)

            def load_b2(v, m):
                row = sample_row(0, v, m, 1)
                if m >= 2:
                    sp.wait_ge(rowbias_done, v + PER * (m - 1))
                sp.dma_start(b2_rows[:, m % 2, :], b2_all[ds(row, 1), :].to_broadcast([P, D])
                             ).then_inc(b2_in[m % 2], 16)

            def load_norm(v, m):
                row0, row1 = sample_row(0, v, m, P), sample_row(1, v, m, P)
                if m >= 2:
                    sp.wait_ge(x1lo_done, v + PER * (m - 1))
                sp.dma_start(gamma_beta[:, m % 2, :], ln_cols[ds(row0, P), :]).then_inc(gamma_beta_in[m % 2], 16)
                sp.dma_start(b[:, m % 2, :], b_cols[ds(row1, P), :]).then_inc(b_in[m % 2], 16)

            sample_loads_at = [(load_w, -2), (load_w1, -10), (load_w2, -9), (load_b1, -8), (load_b2, -6),
                               (load_norm, -3)]

            def step(v, s):
                if in_range(v, s + LOAD_COLS):
                    load_cols(v, s + LOAD_COLS)
                for load, at in sample_loads_at:
                    if (s - at) % PER == 0 and in_range(v, s - at):
                        load(v, (s - at) // PER)
                if in_range(v, s + LOAD_ROWS):
                    load_rows(v, s + LOAD_ROWS)

            FIRST_LOADS = [(load_cols, 0), (load_cols, 1), (load_cols, 2), (load_cols, 3), (load_ids1, 0),
                           (load_w1, 0), (load_cols, 4), (load_w2, 0), (load_cols, 5), (load_b1, 0),
                           (load_cols, 6), (load_b2, 0), (load_rows, 0), (load_cols, 7), (load_rows, 1),
                           (load_rows, 2), (load_w1, 1), (load_cols, 8), (load_rows, 3), (load_w, 0),
                           (load_norm, 0), (load_rows, 4), (load_cols, 9), (load_rows, 5), (load_w2, 1)]
            load_ids0(0, 0)
            for load, i in FIRST_LOADS:
                load(0, i)
            run_steps(sp, 0, 6, TILES, step)
            for k in range(WR):
                sp.wait_ge(stored[k], 16 * (TILES // WR + 1))

        @block.scalar
        def _(act):
            act.wait_ge(eps_done, 1)
            nc.scalar.activation(square_ps[:, 0:1], eps[:], ACT.Sqrt).then_inc(table_loaded, 1)

            def split_cols(v, i):
                act.wait_ge(cols_in[i % XC], slot_loads(v, i, XC))
                act.wait_ge(up_done, v + i - KC + 1)
                nc.scalar.copy(xT_hi[:, i % KC, :], xT[:, i % XC, :]).then_inc(xhi_done, 1)

            def split_w1(v, m):
                act.wait_ge(w1_in, 2 * v + 16 * (m + 1))
                if m >= 2:
                    act.wait_ge(up_done, v + PER * (m - 1))
                nc.scalar.copy(w1_hi[:, m % 2], w1[:]).then_inc(w1hi_done, PER)

            def split_w2(v, m):
                act.wait_ge(w2_in, 2 * v + 16 * (m + 1))
                if m >= 2:
                    act.wait_ge(down_done, v + PER * (m - 1))
                nc.scalar.copy(w2_hi[:, m % 2], w2[:]).then_inc(w2hi_done, PER)

            def split_w(v, m, k):
                if k == 0:
                    act.wait_ge(w_in, 2 * v + 16 * (m + 1))
                nc.scalar.copy(w_hi[:, m % 2, k], w[:, k]).then_inc(whi_done, PER // KC)

            def split_weight(v, table, m, k):
                if table == "w1":
                    split_w1(v, m)
                elif table == "w2":
                    split_w2(v, m)
                else:
                    split_w(v, m, k)

            def relu(v, blk):
                m = blk // 2
                act.wait_ge(up_done, v + BLOCK * (blk + 1))
                if blk % 2 == 0:
                    act.wait_ge(b1_in[m % 2], sample_loads(v, m))
                if blk >= 1:
                    act.wait_ge(hlo_done, v + BLOCK * blk)
                nc.scalar.activation(hT[:], h_ps[:], ACT.Relu, bias=b1[:, m % 2:m % 2 + 1]
                                     ).then_inc(relu_done, BLOCK)
                act.wait_ge(relu_done, v + BLOCK * (blk + 1))
                if blk >= 2:
                    act.wait_ge(down_done, v + BLOCK * (blk - 1))
                nc.scalar.copy(hT_hi[:, blk % 2, :], hT[:]).then_inc(hhi_done, BLOCK)

            def square(v, i):
                r = slice(i % WR, i % WR + 1)
                act.wait_ge(mean_done, v + i + 1)
                act.wait_ge(*((square_done, v + i) if i >= 1 else (table_loaded, 1)))
                nc.scalar.activation(square_ps[:], y[:, i % WR, :], ACT.Square, bias=neg_mean[:, r],
                                     accum_out=sq_sum[:, r]).then_inc(square_done, 1)
                act.wait_ge(square_done, v + i + 1)
                nc.scalar.activation(std[:, r], sq_sum[:, r], ACT.Sqrt, bias=eps[:], scale=1.0 / D
                                     ).then_inc(std_done, 1)

            def normalise(v, i):
                r = slice(i % WR, i % WR + 1)
                act.wait_ge(shift_done, v + i + 1)
                nc.scalar.activation(y[:, i % WR, :], y[:, i % WR, :], ACT.Identity, bias=shift[:, r],
                                     scale=rstd[:, r]).then_inc(norm_done, 1)

            def split_x1(v, i):
                beta = KC + i % KC
                act.wait_ge(x1_done, v + i + 1)
                nc.scalar.activation(x1T_hi[:, i % WR, :], x1T[:, i % WR, :], ACT.Identity,
                                     bias=gamma_beta[:, (i // PER) % 2, beta:beta + 1]).then_inc(x1hi_done, 1)

            def store(v, i):
                act.wait_ge(final_done, v + i + 1)
                first = (i // PER) * D + (i % KC) * P
                half = (i // BLOCK) % 2
                act.dma_start(out_cols[ds(D // PER * v + first, P), half * NB:(half + 1) * NB],
                              x1T[:, i % WR, :]).then_inc(stored[i % WR], 16)

            def step(v, s):
                if s + SPLIT_X >= FIRST_SPLITS and in_range(v, s + SPLIT_X):
                    split_cols(v, s + SPLIT_X)
                if in_range(v, s + MERGE):
                    split_x1(v, s + MERGE)
                if (s + UP) % BLOCK == BLOCK - 1 and in_range(v, s + UP):
                    relu(v, (s + UP) // BLOCK)
                if in_range(v, s + DOWN):
                    square(v, s + DOWN)
                if in_range(v, s + NORM):
                    normalise(v, s + NORM)
                for table, m, k in weight_parts(v, s):
                    split_weight(v, table, m, k)
                if in_range(v, s + FINISH):
                    store(v, s + FINISH)

            run_steps(act, -PER, 9, TILES - 1 - FINISH, step)

        @block.vector
        def _(dve):
            nc.vector.memset(eps[:], EPS).then_inc(eps_done, 1)
            for k in range(WR):
                dve.sem_inc(stored[k], 16)

            def split_cols(v, i):
                if i < FIRST_SPLITS and isinstance(v, int):
                    dve.wait_ge(cols_in[i % XC], slot_loads(v, i, XC))
                    if i >= KC:
                        dve.wait_ge(up_done, i - KC + 1)
                    nc.vector.tensor_copy(xT_hi[:, i % KC, :], xT[:, i % XC, :]).then_inc(first_xhi_done, 1)
                    dve.wait_ge(first_xhi_done, i + 1)
                else:
                    dve.wait_ge(xhi_done, v + i + 1 - FIRST_SPLITS)
                nc.vector.tensor_tensor(xT_lo[:, i % KC, :], xT[:, i % XC, :],
                                        xT_hi[:, i % KC, :].bitcast(f32), ALU.subtract).then_inc(xlo_done, 1)

            def split_h(v, blk):
                dve.wait_ge(hhi_done, v + BLOCK * (blk + 1))
                nc.vector.tensor_tensor(hT_lo[:, blk % 2, :], hT[:], hT_hi[:, blk % 2, :].bitcast(f32),
                                        ALU.subtract).then_inc(hlo_done, BLOCK)

            def add_rows(v, i):
                r = slice(i % WR, i % WR + 1)
                dve.wait_ge(down_done, v + i + 1)
                dve.wait_ge(rowbias_done, v + i + 1)
                if i >= WR:
                    dve.wait_ge(turn_done, v + BLOCK * (i // BLOCK - 1))
                nc.vector.scalar_tensor_tensor(y[:, i % WR, :], down_ps[i % 2][:], 1.0, xrow[:, i % XR, :],
                                               ALU.mult, ALU.add, accum_out=row_sum[:, r]).then_inc(y_done, 1)

            def mean(v, i):
                r = slice(i % WR, i % WR + 1)
                dve.wait_ge(y_done, v + i + 1)
                nc.vector.tensor_scalar(neg_mean[:, r], row_sum[:, r], -1.0 / D, None, ALU.mult
                                        ).then_inc(mean_done, 1)

            def rstd_start(v, i):
                r = slice(i % WR, i % WR + 1)
                dve.wait_ge(std_done, v + i + 1)
                nc.vector.tensor_scalar(neg_half_var[:, r], sq_sum[:, r], -0.5 / D, -0.5 * EPS,
                                        ALU.mult, ALU.add)
                nc.vector.reciprocal(rstd0[:, r], std[:, r]).then_inc(rstd0_done, 1)

            def rstd_newton(v, i):
                r = slice(i % WR, i % WR + 1)
                dve.wait_ge(rstd0_done, v + i + 1)
                nc.vector.scalar_tensor_tensor(newton[:, r], rstd0[:, r], neg_half_var[:, r], rstd0[:, r],
                                               ALU.mult, ALU.mult).then_inc(newton_done, 1)

            def rstd_end(v, i):
                r = slice(i % WR, i % WR + 1)
                dve.wait_ge(newton_done, v + i + 1)
                nc.vector.scalar_tensor_tensor(rstd[:, r], newton[:, r], 1.5, rstd0[:, r],
                                               ALU.add, ALU.mult).then_inc(rstd_done, 1)

            def mean_shift(v, i):
                r = slice(i % WR, i % WR + 1)
                dve.wait_ge(rstd_done, v + i + 1)
                nc.vector.tensor_tensor(shift[:, r], neg_mean[:, r], rstd[:, r], ALU.mult
                                        ).then_inc(shift_done, 1)

            def merge(v, i):
                gamma = i % KC
                dve.wait_ge(turn_done, v + i + 1)
                if i % PER == 0:
                    dve.wait_ge(gamma_beta_in[(i // PER) % 2], sample_loads(v, i // PER))
                dve.wait_ge(stored[i % WR], slot_loads(v, i, WR))
                nc.vector.scalar_tensor_tensor(x1T[:, i % WR, :], turn_ps[i % 2][:],
                                               gamma_beta[:, (i // PER) % 2, gamma:gamma + 1],
                                               xT[:, i % XC, :], ALU.mult, ALU.add).then_inc(x1_done, 1)

            def split_x1(v, i):
                beta = KC + i % KC
                dve.wait_ge(x1hi_done, v + i + 1)
                nc.vector.scalar_tensor_tensor(x1T_lo[:, i % WR, :], x1T[:, i % WR, :],
                                               gamma_beta[:, (i // PER) % 2, beta:beta + 1],
                                               x1T_hi[:, i % WR, :].bitcast(f32),
                                               ALU.add, ALU.subtract).then_inc(x1lo_done, 1)

            def bias_beta(v, m):
                dve.wait_ge(b_in[m % 2], sample_loads(v, m))
                nc.vector.tensor_tensor(b_beta[:, m % 2, :], b[:, m % 2, :], gamma_beta[:, m % 2, KC:],
                                        ALU.add).then_inc(bbeta_done, PER)

            def finish(v, i):
                c = i % KC
                dve.wait_ge(out_done, v + i + 1)
                if i % PER == 0:
                    dve.wait_ge(bbeta_done, v + i + PER)
                nc.vector.scalar_tensor_tensor(x1T[:, i % WR, :], out_ps[i % 2][:],
                                               b_beta[:, (i // PER) % 2, c:c + 1], x1T[:, i % WR, :],
                                               ALU.add, ALU.add).then_inc(final_done, 1)

            def step(v, s):
                if s % PER == 0 and in_range(v, s - PER):
                    bias_beta(v, s // PER - 1)
                if in_range(v, s + MERGE):
                    merge(v, s + MERGE)
                if in_range(v, s + NORM):
                    rstd_start(v, s + NORM)
                if in_range(v, s + DOWN):
                    add_rows(v, s + DOWN)
                if in_range(v, s + NORM):
                    rstd_newton(v, s + NORM)
                if in_range(v, s + DOWN):
                    mean(v, s + DOWN)
                if in_range(v, s + NORM):
                    rstd_end(v, s + NORM)
                if in_range(v, s + MERGE):
                    split_x1(v, s + MERGE)
                if in_range(v, s + NORM):
                    mean_shift(v, s + NORM)
                if in_range(v, s + SPLIT_X_LO):
                    split_cols(v, s + SPLIT_X_LO)
                if isinstance(v, int) and s in FIRST_H_SPLITS:
                    split_h(v, FIRST_H_SPLITS[s])
                if in_range(v, s + FINISH):
                    finish(v, s + FINISH)

            run_steps(dve, -SPLIT_X_LO, 10, TILES - 1 - FINISH, step)

        @block.gpsimd
        def _(pool):
            nc.gpsimd.memset(ident[:], 0.0).then_inc(ident_zero, 1)
            pool.wait_ge(ident_zero, 1)
            nc.gpsimd.affine_select(out=ident[:], in_=ident[:], compare_op=ALU.not_equal, fill=1.0, base=0,
                                    pattern=[[-1, P]], channel_multiplier=1).then_inc(ident_done, 1)

            def bias_rows(v, i):
                m = i // PER
                pool.wait_ge(rows_in[i % XR], slot_loads(v, i, XR))
                if i % PER == 0:
                    pool.wait_ge(b2_in[m % 2], sample_loads(v, m))
                nc.gpsimd.tensor_tensor(xrow[:, i % XR, :], xrow[:, i % XR, :], b2_rows[:, m % 2, :],
                                        ALU.add).then_inc(rowbias_done, 1)

            def split_h(v, blk):
                pool.wait_ge(hhi_done, v + BLOCK * (blk + 1))
                nc.gpsimd.tensor_tensor(hT_lo[:, blk % 2, :], hT[:], hT_hi[:, blk % 2, :].bitcast(f32),
                                        ALU.subtract).then_inc(hlo_done, BLOCK)

            def split_w1(v, m):
                pool.wait_ge(w1hi_done, v + PER * (m + 1))
                nc.gpsimd.tensor_tensor(w1_lo[:, m % 2], w1[:], w1_hi[:, m % 2].bitcast(f32),
                                        ALU.subtract).then_inc(w1lo_done, PER)

            def split_w2(v, m):
                pool.wait_ge(w2hi_done, v + PER * (m + 1))
                nc.gpsimd.tensor_tensor(w2_lo[:, m % 2], w2[:], w2_hi[:, m % 2].bitcast(f32),
                                        ALU.subtract).then_inc(w2lo_done, PER)

            def split_w(v, m, k):
                pool.wait_ge(whi_done, v + PER * m + PER // KC * (k + 1))
                nc.gpsimd.tensor_tensor(w_lo[:, m % 2, k], w[:, k], w_hi[:, m % 2, k].bitcast(f32),
                                        ALU.subtract).then_inc(wlo_done, PER // KC)

            def split_weight(v, table, m, k):
                if table == "w1":
                    split_w1(v, m)
                elif table == "w2":
                    split_w2(v, m)
                else:
                    split_w(v, m, k)

            def step(v, s):
                if (s + UP) % BLOCK == BLOCK - 1 and s + UP >= BLOCK * len(FIRST_H_SPLITS) and in_range(v, s + UP):
                    split_h(v, (s + UP) // BLOCK)
                if in_range(v, s + BIAS_ROWS):
                    bias_rows(v, s + BIAS_ROWS)
                for table, m, k in weight_parts(v, s):
                    split_weight(v, table, m, k)

            run_steps(pool, -PER, 9, TILES - 1, step)

        @block.tensor
        def _(pe):
            WARM_UPS = 14

            def product(out, terms, first=True, last=True):
                for n, (lhsT, rhs) in enumerate(terms):
                    mm = nc.tensor.matmul(out, lhsT, rhs, start=first and n == 0,
                                          stop=last and n == len(terms) - 1)
                return mm

            def up(v, i):
                k, m = i % KC, i // PER
                pe.wait_ge(xlo_done, v + i + 1)
                if i % PER == 0:
                    pe.wait_ge(w1lo_done, v + i + PER)
                if k == 0 and i >= BLOCK:
                    pe.wait_ge(relu_done, v + i)
                hi, lo = w1_hi[:, m % 2, k], w1_lo[:, m % 2, k]
                product(h_ps[:], [(hi, xT_hi[:, k]), (lo, xT_hi[:, k]), (hi, xT_lo[:, k])],
                        first=k == 0, last=k == KC - 1).then_inc(up_done, 1)

            def first_up():
                pe.wait_ge(w1hi_done, PER)
                for k in range(KC):
                    pe.wait_ge(xlo_done, k + 1)
                    product(h_ps[:], [(w1_hi[:, 0, k], xT_hi[:, k]), (w1_hi[:, 0, k], xT_lo[:, k])],
                            first=k == 0, last=False)
                pe.wait_ge(w1lo_done, PER)
                for k in range(KC):
                    product(h_ps[:], [(w1_lo[:, 0, k], xT_hi[:, k])], first=False, last=k == KC - 1
                            ).then_inc(up_done, 1)

            def down(v, i):
                blk, m = i // BLOCK, i // PER
                rows = slice((i % BLOCK) * P, (i % BLOCK + 1) * P)
                if i % BLOCK == 0:
                    pe.wait_ge(hlo_done, v + BLOCK * (blk + 1))
                if i % PER == 0:
                    pe.wait_ge(w2lo_done, v + i + PER)
                if i >= 2:
                    pe.wait_ge(y_done, v + i - 1)
                hi, lo = hT_hi[:, blk % 2, rows], hT_lo[:, blk % 2, rows]
                product(down_ps[i % 2][:], [(hi, w2_hi[:, m % 2]), (hi, w2_lo[:, m % 2]), (lo, w2_hi[:, m % 2])]
                        ).then_inc(down_done, 1)

            def turn(v, i):
                k, blk = i % KC, i // BLOCK
                if k == 0:
                    pe.wait_ge(norm_done, v + BLOCK * (blk + 1))
                if i >= 2:
                    pe.wait_ge(x1_done, v + i - 1)
                for t in range(BLOCK):
                    mm = nc.tensor.transpose(turn_ps[i % 2][:, t * P:(t + 1) * P],
                                             y[:, (blk * BLOCK + t) % WR, k * P:(k + 1) * P], ident[:])
                mm.then_inc(turn_done, 1)

            def out(v, i):
                j, blk, m = i % KC, i // BLOCK, i // PER
                if i % PER == 0:
                    pe.wait_ge(wlo_done, v + i + PER)
                if i >= 2:
                    pe.wait_ge(final_done, v + i - 1)
                cols = slice(j * P, (j + 1) * P)
                x1 = [(blk * BLOCK + k) % WR for k in range(KC)]
                for k in range(KC):
                    if j == 0:
                        pe.wait_ge(x1hi_done, v + BLOCK * blk + k + 1)
                    product(out_ps[i % 2][:], [(part[:, m % 2, k, cols], x1T_hi[:, x1[k]]) for part in (w_hi, w_lo)],
                            first=k == 0, last=False)
                for k in range(KC):
                    if j == 0:
                        pe.wait_ge(x1lo_done, v + BLOCK * blk + k + 1)
                    mm = product(out_ps[i % 2][:], [(w_hi[:, m % 2, k, cols], x1T_lo[:, x1[k]])],
                                 first=False, last=k == KC - 1)
                mm.then_inc(out_done, 1)

            def step(v, s):
                if in_range(v, s + DOWN):
                    down(v, s + DOWN)
                if in_range(v, s + UP):
                    up(v, s + UP)
                if in_range(v, s + OUT):
                    out(v, s + OUT)
                if s + TURN == 0:
                    pe.wait_ge(warmed_up, 1)
                if in_range(v, s + TURN):
                    turn(v, s + TURN)

            pe.wait_ge(ident_done, 1)
            for _ in range(WARM_UPS):
                warm = nc.tensor.matmul(turn_ps[0][:, :P], ident[:], ident[:], start=True, stop=True)
            warm.then_inc(warmed_up, 1)
            first_up()
            run_steps(pe, BLOCK - UP, 11, TILES - 1 - OUT, step)


def kernel(x, itok_B_0_8, itok_B_0_63, L0_cond_W1, L0_cond_b1, L0_cond_W2, L0_cond_b2, L0_cond_gamma,
           L0_cond_beta, L1_cond_W, L1_cond_b):
    import numpy as np
    import concourse.bacc as bacc
    from concourse.bass_utils import run_bass_kernel_spmd

    x, W1, W2, W = (np.asarray(a) for a in (x, L0_cond_W1, L0_cond_W2, L1_cond_W))
    S, R, D = x.shape

    def columns(a):
        a = np.asarray(a)
        return a.reshape(a.shape[0], -1, P).transpose(0, 2, 1).reshape(a.shape[0] * P, -1)

    arrays = {
        "x_rows": x.reshape(S * R, D),
        "x_cols": x.transpose(0, 2, 1).reshape(S * D, R),
        "l0_ids": np.asarray(itok_B_0_8).reshape(1, S),
        "l1_ids": np.asarray(itok_B_0_63).reshape(1, S),
        "w1_all": W1.reshape(-1, W1.shape[-1]),
        "w2_all": W2.reshape(-1, D),
        "b2_all": np.asarray(L0_cond_b2),
        "b1_cols": columns(L0_cond_b1),
        "ln_cols": np.concatenate([columns(L0_cond_gamma), columns(L0_cond_beta)], axis=1),
        "w_all": W.reshape(-1, D),
        "b_cols": columns(L1_cond_b),
    }
    arrays = {n: np.ascontiguousarray(a) for n, a in arrays.items()}
    nc = bacc.Bacc("TRN2", target_bir_lowering=False, num_devices=1)
    args = [nc.dram_tensor(n, a.shape, mybir.dt.from_np(a.dtype), kind="ExternalInput").ap()
            for n, a in arrays.items()]
    out = nc.dram_tensor("out_cols", (S * D, R), mybir.dt.float32, kind="ExternalOutput").ap()
    cond_resid_kernel(nc, *args, out)
    r = run_bass_kernel_spmd(nc, [arrays], core_ids=[0])
    got = r.results[0]["out_cols"]
    return np.ascontiguousarray(got.reshape(S, D, R).transpose(0, 2, 1))
```
